# Optimizing a Trainium2 kernel written in Bass

```python
import numpy as np
import jax
import jax.numpy as jnp

def _softmax(x, axis=-1):
    return jax.nn.softmax(x, axis=axis)

def _gelu(x):
    return jax.nn.gelu(x, approximate=True)

def _silu(x):
    return jax.nn.silu(x)

def _sigmoid(x):
    return jax.nn.sigmoid(x)

def _layernorm(x, axis=-1, eps=1e-05):
    m = jnp.mean(x, axis=axis, keepdims=True)
    v = jnp.var(x, axis=axis, keepdims=True)
    return (x - m) / jnp.sqrt(v + eps)

def _scatter_add(tgt, idx, src, axis=0):
    return tgt.at[idx].add(src)

def _segment_sum(src, seg, n):
    return jax.ops.segment_sum(src, seg, n)
kernel_name = 'mk_cond_resid_d1_seqx_r2_372cbf'

def setup_inputs(seed: int=0):
    np.random.seed(seed)
    _w = jnp.asarray

    def _rec_inputs():
        import jax
        import jax.numpy as jnp
        _rk = jax.random.key(seed)
        x = -0.0003929 + 0.9999 * jax.random.normal(jax.random.fold_in(_rk, 1), (128, 128, 512), jnp.float32)
        _lenS = 128 - jax.random.randint(jax.random.fold_in(_rk, 7), (128,), 0, max(1, 128 // 4) + 1, jnp.int32)
        _lenS2 = 128 - jax.random.randint(jax.random.fold_in(_rk, 8), (128,), 0, max(1, 128 // 4) + 1, jnp.int32)
        cond_1024 = 0.00782532 + 1.00527 * jax.random.normal(jax.random.fold_in(_rk, 11), (128, 512), jnp.float32)
        return (x, cond_1024)
    x, cond_1024 = _rec_inputs()

    def _L0_cond_setup():
        import jax, jax.numpy as jnp
        import numpy as np
        EPS = 1e-08
        key = jax.random.key(seed)
        ks = jax.random.split(key, 8)
        B, S, D, H = (8, 1024, 512, 512)
        scale = 1.0 / np.sqrt(D)
        return {'input_seq': jax.random.normal(ks[0], (B, S, D), dtype=jnp.float32), 'initial_hidden': jax.random.normal(ks[1], (B, H), dtype=jnp.float32), 'W_f': jax.random.normal(ks[2], (H, D), dtype=jnp.float32) * scale, 'b_f': jnp.zeros((H,), dtype=jnp.float32), 'W_i': jax.random.normal(ks[3], (H, D), dtype=jnp.float32) * scale, 'b_i': jnp.zeros((H,), dtype=jnp.float32), 'W_h': jax.random.normal(ks[4], (H, D), dtype=jnp.float32) * scale, 'b_h': jnp.zeros((H,), dtype=jnp.float32)}
    _L0_cond_all = _L0_cond_setup()
    _L0_cond_in = {k: v for k, v in _L0_cond_all.items() if k in ('W_f', 'b_f', 'W_i', 'b_i', 'W_h', 'b_h')}
    del _L0_cond_all
    return {'x': x, 'cond_1024': cond_1024, 'L0_cond_W_f': _L0_cond_in['W_f'], 'L0_cond_b_f': _L0_cond_in['b_f'], 'L0_cond_W_i': _L0_cond_in['W_i'], 'L0_cond_b_i': _L0_cond_in['b_i'], 'L0_cond_W_h': _L0_cond_in['W_h'], 'L0_cond_b_h': _L0_cond_in['b_h']}

def reference(x, cond_1024, L0_cond_W_f, L0_cond_b_f, L0_cond_W_i, L0_cond_b_i, L0_cond_W_h, L0_cond_b_h):
    import jax
    import jax.numpy as jnp

    def _L0_cond_ref(input_seq, initial_hidden, W_f, b_f, W_i, b_i, W_h, b_h):
        import jax, jax.numpy as jnp
        import numpy as np
        EPS = 1e-08
        forget_gate = jax.nn.sigmoid(jnp.einsum('bsd,hd->bsh', input_seq, W_f) + b_f)
        input_gate = jax.nn.sigmoid(jnp.einsum('bsd,hd->bsh', input_seq, W_i) + b_i)
        gate_sum = forget_gate + input_gate + EPS
        forget_norm = forget_gate / gate_sum
        input_norm = input_gate / gate_sum
        candidate = jnp.einsum('bsd,hd->bsh', input_seq, W_h) + b_h
        new_info = input_norm * candidate
        log_ret = jnp.log(forget_norm + EPS)
        log_cumprod = jnp.cumsum(log_ret, axis=1)
        B, _, H = log_cumprod.shape
        padded = jnp.concatenate([jnp.zeros((B, 1, H), dtype=log_cumprod.dtype), log_cumprod], axis=1)
        scaling = jnp.exp(log_cumprod[:, -1:, :] - padded[:, :-1, :])
        hidden = jnp.cumsum(scaling * new_info, axis=1)
        hidden = hidden + jnp.exp(log_cumprod) * initial_hidden[:, None, :]
        return hidden
    x = x + _L0_cond_ref(x, cond_1024, L0_cond_W_f, L0_cond_b_f, L0_cond_W_i, L0_cond_b_i, L0_cond_W_h, L0_cond_b_h)
    return x

_drawn_inputs = setup_inputs


def setup_inputs(seed=0):
    import zlib

    import numpy as np

    out = dict(_drawn_inputs(seed))
    spreads = {'L0_cond_b_f': (0.0, 2.0), 'L0_cond_b_i': (0.0, 2.0), 'L0_cond_b_h': (0.0, 2.0)}
    factors = {'L0_cond_W_f': 3.734, 'L0_cond_W_i': 3.713}
    for name, (base, spread) in spreads.items():
        noise = np.random.default_rng([zlib.crc32(name.encode()), seed]).standard_normal(out[name].shape)
        drawn = base * np.exp(spread * noise) if base else spread * noise
        out[name] = jnp.asarray(drawn.astype(out[name].dtype))
    for name, factor in factors.items():
        out[name] = (out[name] * factor).astype(out[name].dtype)
    return out
```

```python
from contextlib import ExitStack

import concourse.bass as bass
from concourse import mybir

P = 128
F32 = mybir.dt.float32
F32R = mybir.dt.float32r
ALU = mybir.AluOpType
ACT = mybir.ActivationFunctionType

BATCH, TIME, DIM = 128, 128, 512
HIDDEN = 512
GB = 4
GROUPS = BATCH // GB
TOK = GB * TIME
KC = DIM // P
HC = HIDDEN // P
PAD = TIME + 1
SLOTS = 4
EPS = 1e-8
FORGET, INPUT, CAND = range(3)

assert TIME == P and TOK == 512 and GROUPS % SLOTS == 0 and KC == HC == GB == 4


def build(nc, x, cond, w_f, b_f, w_i, b_i, w_h, b_h, out):
    ctx = ExitStack()
    with ctx:

        def sb(name, shape, dt=F32):
            return ctx.enter_context(nc.sbuf_tensor(name, shape, dt))

        def bank(name):
            return ctx.enter_context(nc.psum_tensor(name, [P, TOK], F32))

        def sem(name):
            return ctx.enter_context(nc.semaphore(name))

        x_tile = [sb(f"x_tile{s}", [P, GB, DIM]) for s in range(SLOTS)]
        xt_high = [sb(f"xt_high{s}", [P, KC, TOK], F32R) for s in range(2)]
        xt_low = [sb(f"xt_low{s}", [P, KC, TOK], F32R) for s in range(2)]
        wt_high = sb("wt_high", [P, 3, KC, HIDDEN], F32R)
        wt_low = sb("wt_low", [P, 3, KC, HIDDEN], F32R)
        forget = sb("forget", [P, HC, TOK])
        inp = sb("inp", [P, HC, TOK])
        norm = sb("norm", [P, HC, TOK])
        info = sb("info", [P, HC, TOK])
        log_ret = sb("log_ret", [P, HC, GB * PAD])
        cum_log = sb("cum_log", [P, HC, GB * PAD])
        decay = sb("decay", [P, HC, TOK])
        scaled = sb("scaled", [P, HC, TOK])
        keep_pad = sb("keep_pad", [P, GB * PAD])
        keep = sb("keep", [P, TOK])
        ident = sb("ident", [P, P])
        eps = sb("eps", [P, 1])
        cond_rows = sb("cond_rows", [BATCH, HIDDEN])
        cond_t = sb("cond_t", [P, HC, BATCH])
        cond_group = sb("cond_group", [P, HC, GB])
        bias_rows = sb("bias_rows", [3 * HC, P])
        bias = sb("bias", [P, 3 * HC])
        w_rows = [forget, inp, norm]

        logit_bank = [[bank(f"logits{s}_{k}") for k in range(3)] for s in range(2)]
        xt_bank = bank("xt_bank")
        ht_bank = bank("ht_bank")
        w_banks = [b for s in range(2) for b in logit_bank[s]]

        x_loaded = [sem(f"x_loaded{s}") for s in range(SLOTS)]
        stored = [sem(f"stored{s}") for s in range(SLOTS)]
        w_loaded = [sem(f"w_loaded{k}") for k in range(3)]
        small_loaded = sem("small_loaded")
        consts_zeroed = sem("consts_zeroed")
        ident_ready = sem("ident_ready")
        consts_ready = sem("consts_ready")
        small_transposed = sem("small_transposed")
        small_ready = sem("small_ready")
        w_transposed = sem("w_transposed")
        w_high_ready = sem("w_high_ready")
        w_low_ready = sem("w_low_ready")
        xt_ready = sem("xt_ready")
        x_high_ready = sem("x_high_ready")
        x_low_ready = sem("x_low_ready")
        logits_ready = [sem(f"logits_ready{k}") for k in range(3)]
        forget_ready = sem("forget_ready")
        input_ready = sem("input_ready")
        gate_sum_ready = sem("gate_sum_ready")
        cand_gated = sem("cand_gated")
        log_sum_ready = sem("log_sum_ready")
        recip_ready = sem("recip_ready")
        forget_normed = sem("forget_normed")
        info_ready = sem("info_ready")
        log_ret_ready = sem("log_ret_ready")
        cum_log_ready = sem("cum_log_ready")
        scaling_ready = sem("scaling_ready")
        cond_group_ready = sem("cond_group_ready")
        info_scaled = sem("info_scaled")
        info_summed = sem("info_summed")
        hidden_ready = sem("hidden_ready")
        ht_ready = sem("ht_ready")
        out_ready = sem("out_ready")

        def quarters(it, k, more=0):
            return it * (4 * SLOTS) + (4 * k + more)

        def seg(t, h):
            return t[:, h, :].rearrange("p (b s) -> p b s", s=PAD)

        block = ctx.enter_context(nc.Block())

        @block.sync
        def _(sp):
            def load(it, k):
                s = k % SLOTS
                first = it * (SLOTS * GB) + k * GB
                sp.dma_start(
                    x_tile[s][:, :, :], x[bass.ds(first, GB), :, :].rearrange("b s d -> s b d")
                ).then_inc(x_loaded[s], 16)

            def store(it, k):
                s = k % SLOTS
                first = it * (SLOTS * GB) + k * GB
                sp.wait_ge(out_ready, quarters(it, k, 4))
                sp.dma_start(
                    out[bass.ds(first, GB), :, :].rearrange("b s d -> s b d"), x_tile[s][:, :, :]
                ).then_inc(stored[s], 16)

            def period(it, k, more):
                store(it, k - 1)
                if more:
                    sp.wait_ge(stored[(k - 1) % SLOTS], it * 16 + 16 * ((k - 1) // SLOTS + 1))
                    load(it, k + SLOTS - 1)

            for rows, w, loaded in zip(w_rows, (w_f, w_i, w_h), w_loaded):
                sp.dma_start(rows[:, :, :], w.rearrange("(c p) d -> p c d", p=P)).then_inc(loaded, 16)
                if w is w_f:
                    for k, b in enumerate((b_f, b_i, b_h)):
                        sp.dma_start(
                            bias_rows[k * HC : (k + 1) * HC, :], b.rearrange("(c p) -> c p", p=P)
                        ).then_inc(small_loaded, 16)
                    sp.dma_start(cond_rows[:, :], cond).then_inc(small_loaded, 16)
                    load(0, 0)
            for k in range(1, SLOTS):
                load(0, k)
            with sp.Fori(0, GROUPS // SLOTS - 1) as it:
                for k in range(1, SLOTS + 1):
                    period(it, k, True)
            for k in range(1, SLOTS + 1):
                period(GROUPS // SLOTS - 1, k, False)
            for s in range(SLOTS):
                sp.wait_ge(stored[s], 16 * (GROUPS // SLOTS))

        @block.gpsimd
        def _(pool):
            nc.gpsimd.memset(ident[:, :], 0.0).then_inc(consts_zeroed, 1)
            pool.wait_ge(consts_zeroed, 1)
            nc.gpsimd.affine_select(
                out=ident[:, :], in_=ident[:, :], compare_op=ALU.not_equal, fill=1.0,
                base=0, pattern=[[-1, P]], channel_multiplier=1,
            ).then_inc(ident_ready, 1)

            def period(it, k, first=False):
                for h in range(HC):
                    pool.wait_ge(input_ready, quarters(it, k, h + 1))
                    if not first:
                        pool.wait_ge(info_ready, quarters(it, k, h - 3))
                    nc.gpsimd.tensor_tensor(
                        norm[:, h, :], forget[:, h, :], inp[:, h, :], ALU.add
                    ).then_inc(gate_sum_ready, 1)
                if first:
                    pool.wait_ge(small_ready, 2)
                else:
                    pool.wait_ge(hidden_ready, quarters(it, k))
                nc.gpsimd.tensor_copy(
                    cond_group[:, :, :], cond_t[:, :, bass.ds(it * (SLOTS * GB) + k * GB, GB)]
                ).then_inc(cond_group_ready, 1)

            period(0, 0, first=True)
            with pool.Fori(0, GROUPS // SLOTS - 1) as it:
                for k in range(1, SLOTS + 1):
                    period(it, k)
            for k in range(1, SLOTS):
                period(GROUPS // SLOTS - 1, k)

        @block.scalar
        def _(act):
            def split_high(it, k, c):
                act.wait_ge(xt_ready, quarters(it, k, c + 1))
                nc.scalar.copy(xt_high[k % 2][:, c, :], xt_bank[:, :]).then_inc(x_high_ready, 1)

            def recurrence(it, k, split):
                nc.scalar.preload_act_table_set("natural_log_exp_and_others")
                for h in range(HC):
                    act.wait_ge(gate_sum_ready, quarters(it, k, h + 1))
                    nc.scalar.activation(
                        norm[:, h, :], norm[:, h, :], ACT.Ln, bias=eps[:, 0:1]
                    ).then_inc(log_sum_ready, 1)
                for h in range(HC):
                    act.wait_ge(log_sum_ready, quarters(it, k, h + 1))
                    nc.scalar.activation(
                        norm[:, h, :], norm[:, h, :], ACT.Exp, scale=-1.0
                    ).then_inc(recip_ready, 1)
                if split:
                    split_high(it, k + 2, 0)
                for h in range(HC):
                    act.wait_ge(forget_normed, quarters(it, k, h + 1))
                    nc.scalar.activation(
                        seg(log_ret, h)[:, :, 1:PAD],
                        forget[:, h, :].rearrange("p (b s) -> p b s", s=TIME),
                        ACT.Ln, bias=eps[:, 0:1],
                    ).then_inc(log_ret_ready, 1)
                act.wait_ge(ht_ready, quarters(it, k))
                for h in range(HC):
                    act.wait_ge(cum_log_ready, quarters(it, k, h + 1))
                    cum = seg(cum_log, h)
                    nc.scalar.activation(
                        decay[:, h, :].rearrange("p (b s) -> p b s", s=TIME), cum[:, :, 1:PAD], ACT.Exp
                    )
                    for b in range(GB):
                        last = nc.scalar.activation(
                            scaled[:, h, b * TIME : (b + 1) * TIME], cum[:, b, 0:TIME],
                            ACT.Exp, bias=cum[:, b, TIME:PAD], scale=-1.0,
                        )
                    last.then_inc(scaling_ready, 1)
                if split:
                    split_high(it, k + 2, 1)

            def gates(it, k, split):
                nc.scalar.preload_act_table_set("sigmoid_and_others")
                for h in range(HC):
                    for kind, gate, ready in ((FORGET, forget, forget_ready), (INPUT, inp, input_ready)):
                        act.wait_ge(logits_ready[kind], quarters(it, k, h + 1))
                        nc.scalar.activation(
                            gate[:, h, :], logit_bank[h % 2][kind][:, :], ACT.Sigmoid,
                            bias=bias[:, kind * HC + h : kind * HC + h + 1],
                        ).then_inc(ready, 1)
                    if split and h in (1, 2):
                        split_high(it, k + 1, h + 1)

            act.wait_ge(small_transposed, 1)
            nc.scalar.copy(bias[:, :], ht_bank[:, 0 : 3 * HC]).then_inc(small_ready, 1)
            act.wait_ge(small_transposed, 2)
            nc.scalar.copy(cond_t[:, :, :], xt_bank[:, :]).then_inc(small_ready, 1)
            for n in range(3 * KC):
                act.wait_ge(w_transposed, n + 1)
                nc.scalar.copy(
                    wt_high[:, n // KC, n % KC, :], w_banks[n % 6][:, :]
                ).then_inc(w_high_ready, 1)
                if n >= 8:
                    split_high(0, 0, n - 8)
            for c in range(2):
                split_high(0, 1, c)
            act.wait_ge(consts_ready, 4)
            act.wait_ge(small_ready, 2)
            act.wait_ge(w_low_ready, 3 * KC)
            gates(0, 0, True)
            with act.Fori(0, GROUPS // SLOTS - 1) as it:
                for k in range(1, SLOTS + 1):
                    recurrence(it, k - 1, True)
                    gates(it, k, True)
            last_it = GROUPS // SLOTS - 1
            for k in range(1, SLOTS):
                recurrence(last_it, k - 1, k < SLOTS - 1)
                gates(last_it, k, k < SLOTS - 1)
            recurrence(last_it, SLOTS - 1, False)

        @block.vector
        def _(dve):
            def split_low(it, k, c):
                dve.wait_ge(x_high_ready, quarters(it, k, c + 1))
                nc.vector.tensor_tensor(
                    xt_low[k % 2][:, c, :], xt_bank[:, :], xt_high[k % 2][:, c, :].bitcast(F32),
                    ALU.subtract,
                ).then_inc(x_low_ready, 1)

            def gate_candidate(it, k, h):
                dve.wait_ge(input_ready, quarters(it, k, h + 1))
                dve.wait_ge(logits_ready[CAND], quarters(it, k, h + 1))
                nc.vector.scalar_tensor_tensor(
                    info[:, h, :], logit_bank[h % 2][CAND][:, :],
                    bias[:, CAND * HC + h : CAND * HC + h + 1], inp[:, h, :], ALU.add, ALU.mult,
                ).then_inc(cand_gated, 1)

            def norm_forget(it, k, h):
                dve.wait_ge(recip_ready, quarters(it, k, h + 1))
                nc.vector.tensor_tensor(
                    forget[:, h, :], forget[:, h, :], norm[:, h, :], ALU.mult
                ).then_inc(forget_normed, 1)

            def norm_info(it, k, h):
                dve.wait_ge(cand_gated, quarters(it, k, h + 1))
                nc.vector.tensor_tensor(
                    info[:, h, :], info[:, h, :], norm[:, h, :], ALU.mult
                ).then_inc(info_ready, 1)

            def sum_logs(it, k, h):
                dve.wait_ge(log_ret_ready, quarters(it, k, h + 1))
                nc.vector.tensor_tensor_scan(
                    cum_log[:, h, :], keep_pad[:, :], log_ret[:, h, :], 0.0, ALU.mult, ALU.add
                ).then_inc(cum_log_ready, 1)

            def scale_info(it, k, h):
                dve.wait_ge(scaling_ready, quarters(it, k, h + 1))
                dve.wait_ge(info_ready, quarters(it, k, h + 1))
                nc.vector.tensor_tensor(
                    info[:, h, :], info[:, h, :], scaled[:, h, :], ALU.mult
                ).then_inc(info_scaled, 1)

            def sum_info(it, k, h):
                dve.wait_ge(info_scaled, quarters(it, k, h + 1))
                nc.vector.tensor_tensor_scan(
                    scaled[:, h, :], keep[:, :], info[:, h, :], 0.0, ALU.mult, ALU.add
                ).then_inc(info_summed, 1)

            def add_initial(it, k, h):
                dve.wait_ge(info_summed, quarters(it, k, h + 1))
                for b in range(GB):
                    t = slice(b * TIME, (b + 1) * TIME)
                    last = nc.vector.scalar_tensor_tensor(
                        decay[:, h, t], decay[:, h, t], cond_group[:, h, b : b + 1],
                        scaled[:, h, t], ALU.mult, ALU.add,
                    )
                last.then_inc(hidden_ready, 1)

            def add_x(it, k, b):
                dve.wait_ge(ht_ready, quarters(it, k, b + 1))
                nc.vector.tensor_tensor(
                    x_tile[k % SLOTS][:, b, :], ht_bank[:, :], x_tile[k % SLOTS][:, b, :], ALU.add
                ).then_inc(out_ready, 1)

            def period(it, k, project=True, split=True):
                for h in range(HC):
                    norm_forget(it, k - 1, h)
                if split:
                    split_low(it, k + 1, 0)
                for h in range(HC):
                    norm_info(it, k - 1, h)
                    sum_logs(it, k - 1, h)
                dve.wait_ge(cond_group_ready, it * SLOTS + k)
                scale_info(it, k - 1, 0)
                scale_info(it, k - 1, 1)
                sum_info(it, k - 1, 0)
                sum_info(it, k - 1, 1)
                add_initial(it, k - 1, 0)
                scale_info(it, k - 1, 2)
                add_initial(it, k - 1, 1)
                sum_info(it, k - 1, 2)
                scale_info(it, k - 1, 3)
                if split:
                    split_low(it, k + 1, 1)
                sum_info(it, k - 1, 3)
                add_initial(it, k - 1, 2)
                add_initial(it, k - 1, 3)
                if project:
                    gate_candidate(it, k, 0)
                    gate_candidate(it, k, 1)
                    if split:
                        split_low(it, k + 1, 2)
                    gate_candidate(it, k, 2)
                add_x(it, k - 1, 0)
                if split:
                    split_low(it, k + 1, 3)
                add_x(it, k - 1, 1)
                add_x(it, k - 1, 2)
                if project:
                    gate_candidate(it, k, 3)
                add_x(it, k - 1, 3)

            nc.vector.memset(keep_pad[:, :], 1.0).then_inc(consts_ready, 1)
            nc.vector.memset(keep[:, :], 1.0).then_inc(consts_ready, 1)
            nc.vector.memset(eps[:, :], EPS).then_inc(consts_ready, 1)
            nc.vector.memset(log_ret[:, :, :], 0.0).then_inc(consts_ready, 1)
            dve.wait_ge(consts_ready, 2)
            nc.vector.memset(
                keep_pad[:, :].rearrange("p (b s) -> p b s", s=PAD)[:, :, 0:1], 0.0
            ).then_inc(consts_ready, 1)
            nc.vector.memset(
                keep[:, :].rearrange("p (b s) -> p b s", s=TIME)[:, :, 0:1], 0.0
            ).then_inc(consts_ready, 1)
            for n in range(3 * KC):
                dve.wait_ge(w_high_ready, n + 1)
                w = (slice(None), n // KC, n % KC)
                nc.vector.tensor_tensor(
                    wt_low[w], w_banks[n % 6][:, :], wt_high[w].bitcast(F32), ALU.subtract
                ).then_inc(w_low_ready, 1)
                if n >= 8:
                    split_low(0, 0, n - 8)
            dve.wait_ge(consts_ready, 6)
            dve.wait_ge(small_ready, 2)
            for c in range(2):
                split_low(0, 1, c)
            gate_candidate(0, 0, 0)
            gate_candidate(0, 0, 1)
            split_low(0, 1, 2)
            gate_candidate(0, 0, 2)
            split_low(0, 1, 3)
            gate_candidate(0, 0, 3)
            with dve.Fori(0, GROUPS // SLOTS - 1) as it:
                for k in range(1, SLOTS + 1):
                    period(it, k)
            for k in range(1, SLOTS + 1):
                period(GROUPS // SLOTS - 1, k, project=k < SLOTS, split=k < SLOTS - 1)

        @block.tensor
        def _(pe):
            def transpose_x(it, k, c):
                if c == 0:
                    pe.wait_ge(x_loaded[k % SLOTS], it * 16 + 16 * (k // SLOTS + 1))
                if k or c:
                    pe.wait_ge(x_low_ready, quarters(it, k, c))
                for b in range(GB):
                    last = nc.tensor.transpose(
                        xt_bank[:, b * TIME : (b + 1) * TIME],
                        x_tile[k % SLOTS][:, b, c * P : (c + 1) * P], ident[:, :],
                    )
                last.then_inc(xt_ready, 1)

            def transpose_hidden(it, k, b):
                if b == 0:
                    pe.wait_ge(hidden_ready, quarters(it, k, HC))
                if b:
                    pe.wait_ge(out_ready, quarters(it, k, b))
                for h in range(HC):
                    last = nc.tensor.transpose(
                        ht_bank[:, h * P : (h + 1) * P],
                        decay[:, h, b * TIME : (b + 1) * TIME], ident[:, :],
                    )
                last.then_inc(ht_ready, 1)

            def project(it, k, h, kind, first):
                if h == 0 and kind == FORGET:
                    pe.wait_ge(x_low_ready, quarters(it, k, KC))
                if not first or h >= 2:
                    freed = (forget_ready, input_ready, cand_gated)[kind]
                    pe.wait_ge(freed, quarters(it, k, h - 1))
                high, low = xt_high[k % 2], xt_low[k % 2]
                units = slice(h * P, (h + 1) * P)
                for c in range(KC):
                    for n, (w, xt) in enumerate(((wt_high, high), (wt_high, low), (wt_low, high))):
                        last = nc.tensor.matmul(
                            logit_bank[h % 2][kind][:, :], w[:, kind, c, units], xt[:, c, :],
                            start=c == 0 and n == 0, stop=c == KC - 1 and n == 2,
                        )
                last.then_inc(logits_ready[kind], 1)

            def period(it, k, first=False, project_on=True, split=True):
                for h in range(HC):
                    if project_on:
                        project(it, k, h, FORGET, first)
                    if split:
                        transpose_x(it, k + 1, h)
                    if h == 3 and not first:
                        transpose_hidden(it, k - 1, 1)
                    if project_on:
                        project(it, k, h, INPUT, first)
                    if h == 3 and not first:
                        transpose_hidden(it, k - 1, 2)
                    if project_on:
                        project(it, k, h, CAND, first)
                    if h >= 2 and not first:
                        transpose_hidden(it, k - 1, 0 if h == 2 else 3)

            pe.wait_ge(ident_ready, 1)
            pe.wait_ge(small_loaded, 64)
            nc.tensor.transpose(
                ht_bank[:, 0 : 3 * HC], bias_rows[:, :], ident[0 : 3 * HC, 0 : 3 * HC]
            ).then_inc(small_transposed, 1)
            for h in range(HC):
                last = nc.tensor.transpose(
                    xt_bank[:, h * BATCH : (h + 1) * BATCH], cond_rows[:, h * P : (h + 1) * P], ident[:, :]
                )
            last.then_inc(small_transposed, 1)
            for n in range(3 * KC):
                kind, c = n // KC, n % KC
                if c == 0:
                    pe.wait_ge(w_loaded[kind], 16)
                if n >= 6:
                    pe.wait_ge(w_low_ready, n - 5)
                for h in range(HC):
                    last = nc.tensor.transpose(
                        w_banks[n % 6][:, h * P : (h + 1) * P],
                        w_rows[kind][:, h, c * P : (c + 1) * P], ident[:, :],
                    )
                last.then_inc(w_transposed, 1)
                if n == 8:
                    pe.wait_ge(small_ready, 2)
                if n >= 8:
                    transpose_x(0, 0, n - 8)
            pe.wait_ge(w_low_ready, 3 * KC)
            period(0, 0, first=True)
            with pe.Fori(0, GROUPS // SLOTS - 1) as it:
                for k in range(1, SLOTS + 1):
                    period(it, k)
            for k in range(1, SLOTS + 1):
                period(GROUPS // SLOTS - 1, k, project_on=k < SLOTS, split=k < SLOTS - 1)


_INS = ["x", "cond_1024", "L0_cond_W_f", "L0_cond_b_f", "L0_cond_W_i", "L0_cond_b_i", "L0_cond_W_h", "L0_cond_b_h"]


def kernel(**inputs):
    import numpy as _np
    import concourse.bacc as _bacc
    from concourse import mybir as _mybir
    from concourse.bass_utils import run_bass_kernel_spmd as _run

    nc = _bacc.Bacc("TRN2", target_bir_lowering=False, num_devices=1)
    arrays, args = {}, []
    for name in _INS:
        a = _np.ascontiguousarray(inputs[name])
        arrays[f"in_{name}_dram"] = a
        args.append(nc.dram_tensor(f"in_{name}_dram", a.shape, _mybir.dt.from_np(a.dtype), kind="ExternalInput").ap())
    args.append(nc.dram_tensor("out_0_dram", (BATCH, TIME, DIM), F32, kind="ExternalOutput").ap())
    build(nc, *args)
    r = _run(nc, [arrays], core_ids=[0])
    return r.results[0]["out_0_dram"]
```

```python
from contextlib import ExitStack

import concourse.bass as bass
from concourse import mybir

P = 128
F32 = mybir.dt.float32
F32R = mybir.dt.float32r
ALU = mybir.AluOpType
ACT = mybir.ActivationFunctionType

BATCH, TIME, DIM = 128, 128, 512
HIDDEN = 512
GB = 4
GROUPS = BATCH // GB
TOK = GB * TIME
KC = DIM // P
HC = HIDDEN // P
SQ = 32
NB = P // SQ
PAD = TIME + 1
SLOTS = 4
EPS = 1e-8
FORGET, INPUT, CAND = range(3)

assert TIME == P and TOK == 512 and GROUPS % SLOTS == 0 and KC == HC == GB == 4


def build(nc, x, cond, w_f, b_f, w_i, b_i, w_h, b_h, out):
    ctx = ExitStack()
    with ctx:

        def sb(name, shape, dt=F32):
            return ctx.enter_context(nc.sbuf_tensor(name, shape, dt))

        def bank(name):
            return ctx.enter_context(nc.psum_tensor(name, [P, TOK], F32))

        def sem(name):
            return ctx.enter_context(nc.semaphore(name))

        x_tile = [sb(f"x_tile{s}", [P, GB, DIM]) for s in range(SLOTS)]
        x_turned = [sb(f"x_turned{s}", [P, NB, GB, KC, SQ]) for s in range(2)]
        xt_high = [sb(f"xt_high{s}", [P, NB, GB, KC, SQ], F32R) for s in range(2)]
        xt_low = [sb(f"xt_low{s}", [P, NB, GB, KC, SQ], F32R) for s in range(2)]
        wt_high = sb("wt_high", [P, 3, KC, HIDDEN], F32R)
        wt_low = sb("wt_low", [P, 3, KC, HIDDEN], F32R)
        forget = sb("forget", [P, HC, TOK])
        inp = sb("inp", [P, HC, TOK])
        norm = sb("norm", [P, HC, TOK])
        info = sb("info", [P, HC, TOK])
        log_ret = sb("log_ret", [P, HC, GB * PAD])
        cum_log = sb("cum_log", [P, HC, GB * PAD])
        decay = sb("decay", [P, HC, TOK])
        scaled = sb("scaled", [P, HC, TOK])
        keep_pad = sb("keep_pad", [P, GB * PAD])
        keep = sb("keep", [P, TOK])
        ident = sb("ident", [P, P])
        eps = sb("eps", [P, 1])
        cond_rows = sb("cond_rows", [BATCH, HIDDEN])
        cond_t = sb("cond_t", [P, HC, BATCH])
        cond_group = sb("cond_group", [P, HC, GB])
        bias_rows = sb("bias_rows", [3 * HC, P])
        bias = sb("bias", [P, 3 * HC])
        last_decay = x_tile[GROUPS % SLOTS]
        w_rows = [forget, inp, norm]

        logit_bank = [[bank(f"logits{s}_{k}") for k in range(3)] for s in range(2)]
        ht_bank = [bank(f"ht_bank{s}") for s in range(2)]
        w_banks = [*logit_bank[1], ht_bank[1]]
        first_banks = [ht_bank[0], *logit_bank[0]]
        last_banks = [ht_bank[0], *logit_bank[0]]

        x_loaded = [sem(f"x_loaded{s}") for s in range(SLOTS)]
        stored = [sem(f"stored{s}") for s in range(SLOTS)]
        last_stored = [sem(f"last_stored{b}") for b in range(GB)]
        blocks_turned = sem("blocks_turned")
        blocks_moved = [sem(f"blocks_moved{t}") for t in range(NB)]
        w_loaded = [sem(f"w_loaded{h}") for h in range(HC)]
        small_loaded = [sem("bias_loaded"), sem("cond_loaded")]
        consts_zeroed = sem("consts_zeroed")
        ident_ready = sem("ident_ready")
        consts_ready = sem("consts_ready")
        small_transposed = sem("small_transposed")
        small_ready = sem("small_ready")
        w_transposed = sem("w_transposed")
        w_high_ready = sem("w_high_ready")
        w_low_ready = sem("w_low_ready")
        first_xt_ready = sem("first_xt_ready")
        x_high_ready = sem("x_high_ready")
        x_low_ready = sem("x_low_ready")
        logits_ready = [sem(f"logits_ready{k}") for k in range(3)]
        forget_ready = sem("forget_ready")
        input_ready = sem("input_ready")
        gate_sum_ready = sem("gate_sum_ready")
        cand_gated = sem("cand_gated")
        log_sum_ready = sem("log_sum_ready")
        recip_ready = sem("recip_ready")
        forget_normed = sem("forget_normed")
        info_ready = sem("info_ready")
        log_ret_ready = sem("log_ret_ready")
        cum_log_ready = sem("cum_log_ready")
        scaling_ready = sem("scaling_ready")
        cond_group_ready = sem("cond_group_ready")
        info_scaled = sem("info_scaled")
        info_summed = sem("info_summed")
        hidden_ready = sem("hidden_ready")
        ht_ready = sem("ht_ready")
        out_ready = sem("out_ready")

        def quarters(it, k, more=0):
            return it * (4 * SLOTS) + (4 * k + more)

        def decay_of(last_group):
            return last_decay if last_group else decay

        def chunk(xt, c):
            return xt[:, :, :, c, :].rearrange("p t b i -> p b t i")

        def seg(t, h):
            return t[:, h, :].rearrange("p (b s) -> p b s", s=PAD)

        block = ctx.enter_context(nc.Block())

        @block.sync
        def _(sp):
            def load(it, k):
                s = k % SLOTS
                first = it * (SLOTS * GB) + k * GB
                sp.dma_start(
                    x_tile[s][:, :, :], x[bass.ds(first, GB), :, :].rearrange("b s d -> s b d")
                ).then_inc(x_loaded[s], 16)

            def move_blocks(it, k):
                for t in range(NB):
                    for a in range(NB):
                        sp.dma_start(
                            xt_low[k % 2].bitcast(F32)[a * SQ : (a + 1) * SQ, t, :, :, :],
                            x_turned[k % 2][t * SQ : (t + 1) * SQ, a, :, :, :],
                        ).then_inc(blocks_moved[t], 16)

            def store(it, k):
                s = k % SLOTS
                first = it * (SLOTS * GB) + k * GB
                sp.dma_start(
                    out[bass.ds(first, GB), :, :].rearrange("b s d -> s b d"), x_tile[s][:, :, :]
                ).then_inc(stored[s], 16)

            def store_last(it, k):
                for b in range(GB):
                    sp.wait_ge(out_ready, quarters(it, k, b + 1))
                    sp.dma_start(
                        out[GB * (it * SLOTS + k) + b, :, :], x_tile[k % SLOTS][:, b, :]
                    ).then_inc(last_stored[b], 16)

            def period(it, k, more):
                sp.wait_ge(out_ready, quarters(it, k - 1, 4))
                if more or k < SLOTS - 2:
                    move_blocks(it, k + 2)
                store(it, k - 1)
                if more:
                    sp.wait_ge(stored[(k - 1) % SLOTS], it * 16 + 16 * ((k - 1) // SLOTS + 1))
                    load(it, k + SLOTS - 1)

            def load_weights(h):
                for rows, w in zip(w_rows, (w_f, w_i, w_h)):
                    sp.dma_start(
                        rows[:, h, :], w[h * P : (h + 1) * P, :]
                    ).then_inc(w_loaded[h], 16)

            load_weights(0)
            load(0, 0)
            for k, b in enumerate((b_f, b_i, b_h)):
                sp.dma_start(
                    bias_rows[k * HC : (k + 1) * HC, :], b.rearrange("(c p) -> c p", p=P)
                ).then_inc(small_loaded[0], 16)
            for h in range(1, HC):
                load_weights(h)
            sp.dma_start(cond_rows[:, :], cond).then_inc(small_loaded[1], 16)
            for k in range(1, SLOTS):
                load(0, k)
            sp.wait_ge(blocks_turned, GB)
            move_blocks(0, 1)
            sp.wait_ge(blocks_turned, 2 * GB)
            sp.wait_ge(logits_ready[CAND], HC)
            move_blocks(0, 2)
            with sp.Fori(0, GROUPS // SLOTS - 1) as it:
                for k in range(1, SLOTS + 1):
                    period(it, k, True)
            for k in range(1, SLOTS):
                period(GROUPS // SLOTS - 1, k, False)
            store_last(GROUPS // SLOTS - 1, SLOTS - 1)
            for s in range(SLOTS):
                sp.wait_ge(stored[s], 16 * (GROUPS // SLOTS - (s == SLOTS - 1)))
            for b in range(GB):
                sp.wait_ge(last_stored[b], 16)

        @block.gpsimd
        def _(pool):
            nc.gpsimd.memset(ident[:, :], 0.0).then_inc(consts_zeroed, 1)
            pool.wait_ge(consts_zeroed, 1)
            nc.gpsimd.affine_select(
                out=ident[:, :], in_=ident[:, :], compare_op=ALU.not_equal, fill=1.0,
                base=0, pattern=[[-1, P]], channel_multiplier=1,
            ).then_inc(ident_ready, 1)

            def sum_gates(it, k, h, first=False):
                pool.wait_ge(input_ready, quarters(it, k, h + 1))
                if not first:
                    pool.wait_ge(info_ready, quarters(it, k, h - 3))
                nc.gpsimd.tensor_tensor(
                    norm[:, h, :], forget[:, h, :], inp[:, h, :], ALU.add
                ).then_inc(gate_sum_ready, 1)

            def take_cond(it, k, first=False):
                if first:
                    pool.wait_ge(small_ready, 2)
                else:
                    pool.wait_ge(hidden_ready, quarters(it, k))
                nc.gpsimd.tensor_copy(
                    cond_group[:, :, :], cond_t[:, :, bass.ds(it * (SLOTS * GB) + k * GB, GB)]
                ).then_inc(cond_group_ready, 1)

            def period(it, k, first=False):
                sum_gates(it, k, 0, first)
                sum_gates(it, k, 1, first)
                take_cond(it, k, first)
                sum_gates(it, k, 2, first)
                sum_gates(it, k, 3, first)

            period(0, 0, first=True)
            with pool.Fori(0, GROUPS // SLOTS - 1) as it:
                for k in range(1, SLOTS + 1):
                    period(it, k)
            for k in range(1, SLOTS):
                period(GROUPS // SLOTS - 1, k)

        @block.scalar
        def _(act):
            def split_high(it, k, t):
                act.wait_ge(blocks_moved[t], it * (16 * NB * SLOTS) + 16 * NB * k)
                nc.scalar.copy(
                    xt_high[k % 2][:, t, :, :, :], xt_low[k % 2].bitcast(F32)[:, t, :, :, :]
                ).then_inc(x_high_ready, 1)

            def split_first_high(c):
                act.wait_ge(first_xt_ready, c + 1)
                nc.scalar.copy(
                    chunk(xt_high[0], c),
                    first_banks[c][:, :].rearrange("p (b t i) -> p b t i", t=NB, i=SQ),
                ).then_inc(x_high_ready, 1)

            def recurrence(it, k, split, chunks=range(HC), last_group=False):
                decay = decay_of(last_group)
                nc.scalar.preload_act_table_set("natural_log_exp_and_others")
                for h in chunks:
                    act.wait_ge(gate_sum_ready, quarters(it, k, h + 1))
                    nc.scalar.activation(
                        norm[:, h, :], norm[:, h, :], ACT.Ln, bias=eps[:, 0:1]
                    ).then_inc(log_sum_ready, 1)
                for h in chunks:
                    act.wait_ge(log_sum_ready, quarters(it, k, h + 1))
                    nc.scalar.activation(
                        norm[:, h, :], norm[:, h, :], ACT.Exp, scale=-1.0
                    ).then_inc(recip_ready, 1)
                for h in chunks:
                    act.wait_ge(forget_normed, quarters(it, k, h + 1))
                    nc.scalar.activation(
                        seg(log_ret, h)[:, :, 1:PAD],
                        forget[:, h, :].rearrange("p (b s) -> p b s", s=TIME),
                        ACT.Ln, bias=eps[:, 0:1],
                    ).then_inc(log_ret_ready, 1)
                if split:
                    split_high(it, k + 2, 0)
                if last_group:
                    act.wait_ge(hidden_ready, quarters(it, k))
                    act.wait_ge(stored[GROUPS % SLOTS], 16 * (GROUPS // SLOTS))
                else:
                    act.wait_ge(ht_ready, quarters(it, k))
                for h in chunks:
                    act.wait_ge(cum_log_ready, quarters(it, k, h + 1))
                    cum = seg(cum_log, h)
                    nc.scalar.activation(
                        decay[:, h, :].rearrange("p (b s) -> p b s", s=TIME), cum[:, :, 1:PAD], ACT.Exp
                    )
                    for b in range(GB):
                        last = nc.scalar.activation(
                            scaled[:, h, b * TIME : (b + 1) * TIME], cum[:, b, 0:TIME],
                            ACT.Exp, bias=cum[:, b, TIME:PAD], scale=-1.0,
                        )
                    last.then_inc(scaling_ready, 1)
                    if split and h == 1:
                        split_high(it, k + 2, 1)

            def gates(it, k, split, chunks=range(HC), first=False):
                nc.scalar.preload_act_table_set("sigmoid_and_others")
                for h in chunks:
                    for kind, gate, ready in ((FORGET, forget, forget_ready), (INPUT, inp, input_ready)):
                        act.wait_ge(logits_ready[kind], quarters(it, k, h + 1))
                        nc.scalar.activation(
                            gate[:, h, :], logit_bank[h % 2][kind][:, :], ACT.Sigmoid,
                            bias=bias[:, kind * HC + h : kind * HC + h + 1],
                        ).then_inc(ready, 1)
                        if split and h == 3 and kind == FORGET:
                            split_high(it, k + 1, 3)
                    if first and h < 2:
                        split_high(it, k + 1, h)
                    if split and h == 2:
                        split_high(it, k + 1, 2)

            def weights_high(h):
                for kind in range(3):
                    n = 3 * h + kind
                    act.wait_ge(w_transposed, n + 1)
                    nc.scalar.copy(
                        wt_high[:, kind, :, h * P : (h + 1) * P],
                        w_banks[n % len(w_banks)][:, :].rearrange("p (c u) -> p c u", u=P),
                    ).then_inc(w_high_ready, 1)

            weights_high(0)
            for c in range(KC):
                split_first_high(c)
            weights_high(1)
            act.wait_ge(small_transposed, 1)
            nc.scalar.copy(bias[:, :], logit_bank[0][CAND][:, 0 : 3 * HC]).then_inc(small_ready, 1)
            weights_high(2)
            weights_high(3)
            act.wait_ge(small_transposed, 2)
            nc.scalar.copy(cond_t[:, :, :], logit_bank[0][CAND][:, :]).then_inc(small_ready, 1)
            act.wait_ge(small_ready, 1)
            act.wait_ge(consts_ready, 4)
            act.wait_ge(w_transposed, 3 * HC)
            gates(0, 0, True, first=True)
            with act.Fori(0, GROUPS // SLOTS - 1) as it:
                for k in range(1, SLOTS + 1):
                    recurrence(it, k - 1, True)
                    gates(it, k, True)
            last_it = GROUPS // SLOTS - 1
            for k in range(1, SLOTS - 1):
                recurrence(last_it, k - 1, True)
                gates(last_it, k, True)
            recurrence(last_it, SLOTS - 2, False)
            for chunks in ((0, 1), (2, 3)):
                gates(last_it, SLOTS - 1, False, chunks)
                recurrence(last_it, SLOTS - 1, False, chunks, last_group=True)

        @block.vector
        def _(dve):
            def turn_blocks(it, k, b):
                if b == 0:
                    s = k % SLOTS
                    dve.wait_ge(x_loaded[s], it * 16 + 16 * (k // SLOTS + 1))
                nc.vector.transpose(
                    x_turned[k % 2][:, :, b, :, :].rearrange("p a c i -> p c a i"),
                    x_tile[k % SLOTS][:, b, :].rearrange("p (c a d) -> p c a d", c=KC, d=SQ),
                ).then_inc(blocks_turned, 1)

            def split_low(it, k, t):
                dve.wait_ge(x_high_ready, quarters(it, k, t + 1))
                nc.vector.tensor_tensor(
                    xt_low[k % 2][:, t, :, :, :], xt_low[k % 2].bitcast(F32)[:, t, :, :, :],
                    xt_high[k % 2].bitcast(F32)[:, t, :, :, :], ALU.subtract,
                ).then_inc(x_low_ready, 1)

            def split_first_low(c):
                dve.wait_ge(x_high_ready, c + 1)
                nc.vector.tensor_tensor(
                    chunk(xt_low[0], c),
                    first_banks[c][:, :].rearrange("p (b t i) -> p b t i", t=NB, i=SQ),
                    chunk(xt_high[0].bitcast(F32), c), ALU.subtract,
                ).then_inc(x_low_ready, 1)

            def gate_candidate(it, k, h):
                dve.wait_ge(input_ready, quarters(it, k, h + 1))
                dve.wait_ge(logits_ready[CAND], quarters(it, k, h + 1))
                nc.vector.scalar_tensor_tensor(
                    info[:, h, :], logit_bank[h % 2][CAND][:, :],
                    bias[:, CAND * HC + h : CAND * HC + h + 1], inp[:, h, :], ALU.add, ALU.mult,
                ).then_inc(cand_gated, 1)

            def norm_forget(it, k, h):
                dve.wait_ge(recip_ready, quarters(it, k, h + 1))
                nc.vector.tensor_tensor(
                    forget[:, h, :], forget[:, h, :], norm[:, h, :], ALU.mult
                ).then_inc(forget_normed, 1)

            def norm_info(it, k, h):
                dve.wait_ge(cand_gated, quarters(it, k, h + 1))
                nc.vector.tensor_tensor(
                    info[:, h, :], info[:, h, :], norm[:, h, :], ALU.mult
                ).then_inc(info_ready, 1)

            def sum_logs(it, k, h):
                dve.wait_ge(log_ret_ready, quarters(it, k, h + 1))
                nc.vector.tensor_tensor_scan(
                    cum_log[:, h, :], keep_pad[:, :], log_ret[:, h, :], 0.0, ALU.mult, ALU.add
                ).then_inc(cum_log_ready, 1)

            def scale_info(it, k, h):
                dve.wait_ge(scaling_ready, quarters(it, k, h + 1))
                dve.wait_ge(info_ready, quarters(it, k, h + 1))
                nc.vector.tensor_tensor(
                    info[:, h, :], info[:, h, :], scaled[:, h, :], ALU.mult
                ).then_inc(info_scaled, 1)

            def sum_info(it, k, h):
                dve.wait_ge(info_scaled, quarters(it, k, h + 1))
                nc.vector.tensor_tensor_scan(
                    scaled[:, h, :], keep[:, :], info[:, h, :], 0.0, ALU.mult, ALU.add
                ).then_inc(info_summed, 1)

            def add_initial(it, k, h, last_group=False):
                decay = decay_of(last_group)
                dve.wait_ge(info_summed, quarters(it, k, h + 1))
                for b in range(GB):
                    t = slice(b * TIME, (b + 1) * TIME)
                    last = nc.vector.scalar_tensor_tensor(
                        decay[:, h, t], decay[:, h, t], cond_group[:, h, b : b + 1],
                        scaled[:, h, t], ALU.mult, ALU.add,
                    )
                last.then_inc(hidden_ready, 1)

            def add_x(it, k, b, source=None):
                source = source or ht_bank[b % 2]
                dve.wait_ge(ht_ready, quarters(it, k, b + 1))
                nc.vector.tensor_tensor(
                    x_tile[k % SLOTS][:, b, :], source[:, :], x_tile[k % SLOTS][:, b, :], ALU.add
                ).then_inc(out_ready, 1)

            def period(it, k, split=True, last=False, more=True):

                def turn_next(b):
                    if more:
                        turn_blocks(it, k + 2, b)

                for h in range(HC):
                    norm_forget(it, k - 1, h)
                for h in range(HC):
                    norm_info(it, k - 1, h)
                    sum_logs(it, k - 1, h)
                if split:
                    split_low(it, k + 1, 0)
                dve.wait_ge(cond_group_ready, it * SLOTS + k)
                scale_info(it, k - 1, 0)
                scale_info(it, k - 1, 1)
                sum_info(it, k - 1, 0)
                sum_info(it, k - 1, 1)
                add_initial(it, k - 1, 0)
                scale_info(it, k - 1, 2)
                add_initial(it, k - 1, 1)
                gate_candidate(it, k, 0)
                sum_info(it, k - 1, 2)
                scale_info(it, k - 1, 3)
                sum_info(it, k - 1, 3)
                add_initial(it, k - 1, 2)
                add_initial(it, k - 1, 3)
                if split:
                    split_low(it, k + 1, 1)
                    turn_next(0)
                gate_candidate(it, k, 1)
                if last:
                    half_recurrence(it, k, 0, (0, 1, 2, 3))
                    half_recurrence(it, k, 2, ())
                    return
                gate_candidate(it, k, 2)
                split_low(it, k + 1, 2)
                turn_next(1)
                add_x(it, k - 1, 0)
                split_low(it, k + 1, 3)
                turn_next(2)
                add_x(it, k - 1, 1)
                turn_next(3)
                add_x(it, k - 1, 2)
                gate_candidate(it, k, 3)
                add_x(it, k - 1, 3)

            def half_recurrence(it, k, h, added):
                added = iter(added)

                def add_next():
                    for b in added:
                        add_x(it, k - 1, b)
                        return

                norm_forget(it, k, h)
                norm_forget(it, k, h + 1)
                for n in (h, h + 1):
                    if h:
                        gate_candidate(it, k, n)
                    sum_logs(it, k, n)
                for n in (h, h + 1):
                    norm_info(it, k, n)
                    add_next()
                dve.wait_ge(cond_group_ready, it * SLOTS + (k + 1))
                for n in (h, h + 1):
                    scale_info(it, k, n)
                    sum_info(it, k, n)
                    add_initial(it, k, n, last_group=True)
                    add_next()

            nc.vector.memset(keep_pad[:, :], 1.0).then_inc(consts_ready, 1)
            nc.vector.memset(keep[:, :], 1.0).then_inc(consts_ready, 1)
            nc.vector.memset(eps[:, :], EPS).then_inc(consts_ready, 1)
            nc.vector.memset(
                log_ret[:, :, :].rearrange("p h (b s) -> p (h b) s", s=PAD)[:, :, 0:1], 0.0
            ).then_inc(consts_ready, 1)
            dve.wait_ge(consts_ready, 2)
            nc.vector.memset(
                keep_pad[:, :].rearrange("p (b s) -> p b s", s=PAD)[:, :, 0:1], 0.0
            ).then_inc(consts_ready, 1)
            nc.vector.memset(
                keep[:, :].rearrange("p (b s) -> p b s", s=TIME)[:, :, 0:1], 0.0
            ).then_inc(consts_ready, 1)
            def weights_low(h):
                for kind in range(3):
                    n = 3 * h + kind
                    dve.wait_ge(w_high_ready, n + 1)
                    w = (slice(None), kind, slice(None), slice(h * P, (h + 1) * P))
                    nc.vector.tensor_tensor(
                        wt_low[w], w_banks[n % len(w_banks)][:, :].rearrange("p (c u) -> p c u", u=P),
                        wt_high[w].bitcast(F32), ALU.subtract,
                    ).then_inc(w_low_ready, 1)

            weights_low(0)
            for c in range(KC):
                split_first_low(c)
            for h in range(1, HC):
                weights_low(h)
            for b in range(GB):
                turn_blocks(0, 1, b)
            dve.wait_ge(consts_ready, 6)
            dve.wait_ge(small_ready, 1)
            for h in range(HC):
                gate_candidate(0, 0, h)
                split_low(0, 1, h)
                turn_blocks(0, 2, h)
            with dve.Fori(0, GROUPS // SLOTS - 1) as it:
                for k in range(1, SLOTS + 1):
                    period(it, k)
            last_it = GROUPS // SLOTS - 1
            period(last_it, 1)
            period(last_it, 2, more=False)
            period(last_it, 3, split=False, last=True)
            for b in range(GB):
                add_x(last_it, SLOTS - 1, b, last_banks[b])

        @block.tensor
        def _(pe):
            def transpose_first_x(c):
                for b in range(GB):
                    last = nc.tensor.transpose(
                        first_banks[c][:, b * TIME : (b + 1) * TIME],
                        x_tile[0][:, b, c * P : (c + 1) * P], ident[:, :],
                    )
                last.then_inc(first_xt_ready, 1)

            def transpose_hidden(it, k, b):
                if b == 0:
                    pe.wait_ge(hidden_ready, quarters(it, k, HC))
                if b >= 2:
                    pe.wait_ge(out_ready, quarters(it, k, b - 1))
                for h in range(HC):
                    last = nc.tensor.transpose(
                        ht_bank[b % 2][:, h * P : (h + 1) * P],
                        decay[:, h, b * TIME : (b + 1) * TIME], ident[:, :],
                    )
                last.then_inc(ht_ready, 1)

            def project(it, k, h, kind, first=False, part=(0, 1, 2, 3)):
                if h == 0 and kind == FORGET:
                    pe.wait_ge(x_low_ready, quarters(it, k, KC))
                if first and h == 0:
                    pe.wait_ge(w_low_ready, kind + 1)
                if first and h == 1:
                    pe.wait_ge(w_low_ready, 3 * HC)
                if part[0] == 0 and (not first or h >= 2):
                    freed = (forget_ready, input_ready, cand_gated)[kind]
                    pe.wait_ge(freed, quarters(it, k, h - 1))
                high, low = xt_high[k % 2], xt_low[k % 2]
                units = slice(h * P, (h + 1) * P)
                for c in part:
                    for n, (w, xt) in enumerate(((wt_high, high), (wt_high, low), (wt_low, high))):
                        last = nc.tensor.matmul(
                            logit_bank[h % 2][kind][:, :], w[:, kind, c, units], chunk(xt, c),
                            start=c == 0 and n == 0, stop=c == KC - 1 and n == 2,
                        )
                if part[-1] == KC - 1:
                    last.then_inc(logits_ready[kind], 1)

            def period(it, k):
                for h in range(HC):
                    project(it, k, h, FORGET)
                    if h == 3:
                        transpose_hidden(it, k - 1, 0)
                    project(it, k, h, INPUT)
                    if h == 3:
                        transpose_hidden(it, k - 1, 1)
                        project(it, k, h, CAND, part=(0, 1))
                        transpose_hidden(it, k - 1, 2)
                        project(it, k, h, CAND, part=(2, 3))
                        transpose_hidden(it, k - 1, 3)
                    else:
                        project(it, k, h, CAND)

            def transpose_weights(h):
                pe.wait_ge(w_loaded[h], 48)
                for kind in range(3):
                    n = 3 * h + kind
                    if n >= len(w_banks):
                        pe.wait_ge(w_low_ready, n - len(w_banks) + 1)
                    for c in range(KC):
                        last = nc.tensor.transpose(
                            w_banks[n % len(w_banks)][:, c * P : (c + 1) * P],
                            w_rows[kind][:, h, c * P : (c + 1) * P], ident[:, :],
                        )
                    last.then_inc(w_transposed, 1)

            pe.wait_ge(ident_ready, 1)
            transpose_weights(0)
            pe.wait_ge(x_loaded[0], 16)
            for c in range(KC):
                transpose_first_x(c)
            transpose_weights(1)
            pe.wait_ge(x_low_ready, KC)
            pe.wait_ge(small_loaded[0], 48)
            nc.tensor.transpose(
                logit_bank[0][CAND][:, 0 : 3 * HC], bias_rows[:, :], ident[0 : 3 * HC, 0 : 3 * HC]
            ).then_inc(small_transposed, 1)
            project(0, 0, 0, FORGET, first=True)
            transpose_weights(2)
            project(0, 0, 0, INPUT, first=True)
            transpose_weights(3)
            pe.wait_ge(small_loaded[1], 16)
            pe.wait_ge(small_ready, 1)
            for h in range(HC):
                last = nc.tensor.transpose(
                    logit_bank[0][CAND][:, h * BATCH : (h + 1) * BATCH],
                    cond_rows[:, h * P : (h + 1) * P], ident[:, :],
                )
            last.then_inc(small_transposed, 1)
            pe.wait_ge(small_ready, 2)
            project(0, 0, 0, CAND, first=True)
            for h in range(1, HC):
                project(0, 0, h, FORGET, first=True)
                project(0, 0, h, INPUT, first=True)
                project(0, 0, h, CAND, first=True)
            with pe.Fori(0, GROUPS // SLOTS - 1) as it:
                for k in range(1, SLOTS + 1):
                    period(it, k)
            last_it = GROUPS // SLOTS - 1
            period(last_it, 1)
            period(last_it, 2)
            k = SLOTS - 1
            for h in range(2):
                for kind in (FORGET, INPUT, CAND):
                    project(last_it, k, h, kind)
            for h in range(2, HC):
                project(last_it, k, h, FORGET)
                transpose_hidden(last_it, k - 1, 2 * h - 4)
                project(last_it, k, h, INPUT)
                transpose_hidden(last_it, k - 1, 2 * h - 3)
            for h in range(2, HC):
                project(last_it, k, h, CAND)
            pe.wait_ge(cand_gated, quarters(last_it, k, HC))
            pe.wait_ge(out_ready, quarters(last_it, k))
            for h in range(HC):
                if h >= HC - 2:
                    pe.wait_ge(hidden_ready, quarters(last_it, k, h + 1))
                elif h == 0:
                    pe.wait_ge(hidden_ready, quarters(last_it, k, HC - 2))
                for b in range(GB):
                    last = nc.tensor.transpose(
                        last_banks[b][:, h * P : (h + 1) * P],
                        last_decay[:, h, b * TIME : (b + 1) * TIME], ident[:, :],
                    )
                    if h == HC - 1:
                        last.then_inc(ht_ready, 1)


_INS = ["x", "cond_1024", "L0_cond_W_f", "L0_cond_b_f", "L0_cond_W_i", "L0_cond_b_i", "L0_cond_W_h", "L0_cond_b_h"]


def kernel(**inputs):
    import numpy as _np
    import concourse.bacc as _bacc
    from concourse import mybir as _mybir
    from concourse.bass_utils import run_bass_kernel_spmd as _run

    nc = _bacc.Bacc("TRN2", target_bir_lowering=False, num_devices=1)
    arrays, args = {}, []
    for name in _INS:
        a = _np.ascontiguousarray(inputs[name])
        arrays[f"in_{name}_dram"] = a
        args.append(nc.dram_tensor(f"in_{name}_dram", a.shape, _mybir.dt.from_np(a.dtype), kind="ExternalInput").ap())
    args.append(nc.dram_tensor("out_0_dram", (BATCH, TIME, DIM), F32, kind="ExternalOutput").ap())
    build(nc, *args)
    r = _run(nc, [arrays], core_ids=[0])
    return r.results[0]["out_0_dram"]
```

```python
from contextlib import ExitStack

import concourse.bass as bass
from concourse import mybir

P = 128
F32 = mybir.dt.float32
F32R = mybir.dt.float32r
ALU = mybir.AluOpType
ACT = mybir.ActivationFunctionType

BATCH, TIME, DIM = 128, 128, 512
HIDDEN = 512
GB = 4
GROUPS = BATCH // GB
TOK = GB * TIME
KC = DIM // P
HC = HIDDEN // P
SQ = 32
NB = P // SQ
PAD = TIME + 1
SLOTS = 4
EPS = 1e-8
FORGET, INPUT, CAND = range(3)

assert TIME == P and TOK == 512 and GROUPS % SLOTS == 0 and KC == HC == GB == 4


def build(nc, x, cond, w_f, b_f, w_i, b_i, w_h, b_h, out):
    ctx = ExitStack()
    with ctx:

        def sb(name, shape, dt=F32):
            return ctx.enter_context(nc.sbuf_tensor(name, shape, dt))

        def bank(name):
            return ctx.enter_context(nc.psum_tensor(name, [P, TOK], F32))

        def sem(name):
            return ctx.enter_context(nc.semaphore(name))

        x_tile = [sb(f"x_tile{s}", [P, GB, DIM]) for s in range(SLOTS)]
        x_turned = sb("x_turned", [P, NB, GB, KC, SQ])
        xt_high = [sb(f"xt_high{s}", [P, NB, GB, KC, SQ], F32R) for s in range(2)]
        xt_low = [sb(f"xt_low{s}", [P, NB, GB, KC, SQ], F32R) for s in range(2)]
        wt_high = sb("wt_high", [P, 3, KC, HIDDEN], F32R)
        wt_low = sb("wt_low", [P, 3, KC, HIDDEN], F32R)
        hidden_turned = sb("hidden_turned", [P, NB, GB, HC, SQ])
        hidden_moved = sb("hidden_moved", [P, NB, GB, HC, SQ])
        forget = sb("forget", [P, HC, TOK])
        inp = sb("inp", [P, HC, TOK])
        norm = sb("norm", [P, HC, TOK])
        info = sb("info", [P, HC, TOK])
        log_ret = sb("log_ret", [P, HC, GB * PAD])
        cum_log = sb("cum_log", [P, HC, GB * PAD])
        decay = sb("decay", [P, HC, TOK])
        scaled = sb("scaled", [P, HC, TOK])
        keep_pad = sb("keep_pad", [P, GB * PAD])
        keep = sb("keep", [P, TOK])
        ident = sb("ident", [P, P])
        eps = sb("eps", [P, 1])
        cond_t = sb("cond_t", [P, HC, BATCH])
        cond_group = sb("cond_group", [P, HC, GB])
        bias_rows = sb("bias_rows", [3 * HC, P])
        bias = sb("bias", [P, 3 * HC])
        last_decay = x_tile[GROUPS % SLOTS]
        w_rows = [forget, inp, norm]
        cond_rows = scaled[:, 0, :]

        logit_bank = [[bank(f"logits{s}_{k}") for k in range(3)] for s in range(2)]
        spare_bank = [bank(f"spare_bank{s}") for s in range(2)]
        w_banks = [*logit_bank[1], spare_bank[1]]
        first_banks = [spare_bank[0], *logit_bank[0]]
        small_bank = spare_bank[0]
        last_banks = [spare_bank[0], *logit_bank[0]]

        x_loaded = [sem(f"x_loaded{s}") for s in range(SLOTS)]
        stored = [sem(f"stored{s}") for s in range(SLOTS)]
        last_stored = [sem(f"last_stored{b}") for b in range(GB)]
        blocks_turned = sem("blocks_turned")
        blocks_moved = [sem(f"blocks_moved{t}") for t in range(NB)]
        w_loaded = [sem(f"w_loaded{h}") for h in range(HC)]
        small_loaded = [sem("bias_loaded"), sem("cond_loaded")]
        consts_zeroed = sem("consts_zeroed")
        ident_ready = sem("ident_ready")
        consts_ready = sem("consts_ready")
        small_transposed = sem("small_transposed")
        small_ready = sem("small_ready")
        w_transposed = sem("w_transposed")
        w_high_ready = sem("w_high_ready")
        w_low_ready = sem("w_low_ready")
        first_xt_ready = sem("first_xt_ready")
        x_high_ready = sem("x_high_ready")
        x_low_ready = sem("x_low_ready")
        logits_ready = [sem(f"logits_ready{k}") for k in range(3)]
        forget_ready = sem("forget_ready")
        input_ready = sem("input_ready")
        gate_sum_ready = sem("gate_sum_ready")
        cand_gated = sem("cand_gated")
        log_sum_ready = sem("log_sum_ready")
        recip_ready = sem("recip_ready")
        forget_normed = sem("forget_normed")
        info_ready = sem("info_ready")
        log_ret_ready = sem("log_ret_ready")
        cum_log_ready = sem("cum_log_ready")
        scaling_ready = sem("scaling_ready")
        cond_group_ready = sem("cond_group_ready")
        info_scaled = sem("info_scaled")
        info_summed = sem("info_summed")
        hidden_ready = sem("hidden_ready")
        hidden_blocks_turned = sem("hidden_blocks_turned")
        hidden_blocks_moved = [sem(f"hidden_blocks_moved{s}") for s in range(2)]
        ht_ready = sem("ht_ready")
        out_ready = sem("out_ready")

        def quarters(it, k, more=0):
            return it * (4 * SLOTS) + (4 * k + more)

        def bank_of(h, kind, last_group):
            if h == 2 and kind != CAND and not last_group:
                return spare_bank[kind]
            return logit_bank[h % 2][kind]

        def decay_of(last_group):
            return last_decay if last_group else decay

        def chunk(xt, c):
            return xt[:, :, :, c, :].rearrange("p t b i -> p b t i")

        def seg(t, h):
            return t[:, h, :].rearrange("p (b s) -> p b s", s=PAD)

        block = ctx.enter_context(nc.Block())

        @block.sync
        def _(sp):
            def load(it, k):
                s = k % SLOTS
                first = it * (SLOTS * GB) + k * GB
                sp.dma_start(
                    x_tile[s][:, :, :], x[bass.ds(first, GB), :, :].rearrange("b s d -> s b d")
                ).then_inc(x_loaded[s], 16)

            def move_blocks(it, k):
                for t in range(NB):
                    for a in range(NB):
                        sp.dma_start(
                            xt_low[k % 2].bitcast(F32)[a * SQ : (a + 1) * SQ, t, :, :, :],
                            x_turned[t * SQ : (t + 1) * SQ, a, :, :, :],
                        ).then_inc(blocks_moved[t], 16)

            def move_hidden(it, k):
                sp.wait_ge(hidden_blocks_turned, quarters(it, k, HC))
                for t in range(NB):
                    for u in range(NB):
                        sp.dma_start(
                            hidden_moved[t * SQ : (t + 1) * SQ, u, :, :, :],
                            hidden_turned[u * SQ : (u + 1) * SQ, t, :, :, :],
                        ).then_inc(hidden_blocks_moved[k % 2], 16)

            def store(it, k):
                s = k % SLOTS
                first = it * (SLOTS * GB) + k * GB
                sp.wait_ge(out_ready, quarters(it, k, 4))
                sp.dma_start(
                    out[bass.ds(first, GB), :, :].rearrange("b s d -> s b d"), x_tile[s][:, :, :]
                ).then_inc(stored[s], 16)

            def store_last(it, k):
                for b in range(GB):
                    sp.wait_ge(out_ready, quarters(it, k, b + 1))
                    sp.dma_start(
                        out[GB * (it * SLOTS + k) + b, :, :], x_tile[k % SLOTS][:, b, :]
                    ).then_inc(last_stored[b], 16)

            def period(it, k, first=False, more=True):
                sp.wait_ge(cand_gated, quarters(it, k))
                move_blocks(it, k + 1)
                if not first:
                    store(it, k - 2)
                if not first and more:
                    sp.wait_ge(stored[(k - 2) % SLOTS], it * 16 + 16 * ((k - 2) // SLOTS + 1))
                    load(it, k + SLOTS - 2)
                move_hidden(it, k - 1)

            def load_weights(h):
                for rows, w in zip(w_rows, (w_f, w_i, w_h)):
                    sp.dma_start(
                        rows[:, h, :], w[h * P : (h + 1) * P, :]
                    ).then_inc(w_loaded[h], 16)

            load_weights(0)
            load(0, 0)
            for k, b in enumerate((b_f, b_i, b_h)):
                sp.dma_start(
                    bias_rows[k * HC : (k + 1) * HC, :], b.rearrange("(c p) -> c p", p=P)
                ).then_inc(small_loaded[0], 16)
            for h in range(1, HC):
                load_weights(h)
            sp.dma_start(cond_rows, cond).then_inc(small_loaded[1], 16)
            for k in range(1, SLOTS):
                load(0, k)
            sp.wait_ge(blocks_turned, GB)
            move_blocks(0, 1)
            period(0, 1, first=True)
            with sp.Fori(0, GROUPS // SLOTS - 1) as it:
                for k in range(2, SLOTS + 2):
                    period(it, k)
            last_it = GROUPS // SLOTS - 1
            period(last_it, SLOTS - 2, more=False)
            store(last_it, SLOTS - 3)
            store(last_it, SLOTS - 2)
            store_last(last_it, SLOTS - 1)
            for s in range(SLOTS):
                sp.wait_ge(stored[s], 16 * (GROUPS // SLOTS - (s == SLOTS - 1)))
            for b in range(GB):
                sp.wait_ge(last_stored[b], 16)

        @block.gpsimd
        def _(pool):
            nc.gpsimd.memset(ident[:, :], 0.0).then_inc(consts_zeroed, 1)
            pool.wait_ge(consts_zeroed, 1)
            nc.gpsimd.affine_select(
                out=ident[:, :], in_=ident[:, :], compare_op=ALU.not_equal, fill=1.0,
                base=0, pattern=[[-1, P]], channel_multiplier=1,
            ).then_inc(ident_ready, 1)

            def sum_gates(it, k, h, first=False):
                pool.wait_ge(input_ready, quarters(it, k, h + 1))
                if not first:
                    pool.wait_ge(info_ready, quarters(it, k, h - 3))
                nc.gpsimd.tensor_tensor(
                    norm[:, h, :], forget[:, h, :], inp[:, h, :], ALU.add
                ).then_inc(gate_sum_ready, 1)

            def norm_info(it, k, h):
                pool.wait_ge(recip_ready, quarters(it, k, h + 1))
                pool.wait_ge(cand_gated, quarters(it, k, h + 1))
                nc.gpsimd.tensor_tensor(
                    info[:, h, :], info[:, h, :], norm[:, h, :], ALU.mult
                ).then_inc(info_ready, 1)

            def split_low(it, k, t):
                pool.wait_ge(x_high_ready, quarters(it, k, t + 1))
                nc.gpsimd.tensor_tensor(
                    xt_low[k % 2][:, t, :, :, :], xt_low[k % 2].bitcast(F32)[:, t, :, :, :],
                    xt_high[k % 2].bitcast(F32)[:, t, :, :, :], ALU.subtract,
                ).then_inc(x_low_ready, 1)

            def take_cond(it, k, first=False):
                if first:
                    pool.wait_ge(small_ready, 2)
                else:
                    pool.wait_ge(hidden_ready, quarters(it, k))
                nc.gpsimd.tensor_copy(
                    cond_group[:, :, :], cond_t[:, :, bass.ds(it * (SLOTS * GB) + k * GB, GB)]
                ).then_inc(cond_group_ready, 1)

            def period(it, k, first=False, last=False):
                if not first:
                    for h in range(HC):
                        norm_info(it, k - 1, h)
                for h in range(2):
                    sum_gates(it, k, h, first)
                    if not last:
                        split_low(it, k + 1, h)
                if not last:
                    split_low(it, k + 1, 2)
                    split_low(it, k + 1, 3)
                if last:
                    norm_info(it, k, 0)
                    norm_info(it, k, 1)
                take_cond(it, k, first)
                sum_gates(it, k, 2, first)
                sum_gates(it, k, 3, first)
                if last:
                    norm_info(it, k, 2)
                    norm_info(it, k, 3)

            period(0, 0, first=True)
            period(0, 1)
            with pool.Fori(0, GROUPS // SLOTS - 1) as it:
                for k in range(2, SLOTS + 2):
                    period(it, k)
            for k in range(2, SLOTS):
                period(GROUPS // SLOTS - 1, k, last=k == SLOTS - 1)

        @block.scalar
        def _(act):
            def split_high(it, k, t):
                act.wait_ge(blocks_moved[t], it * (16 * NB * SLOTS) + 16 * NB * k)
                nc.scalar.copy(
                    xt_high[k % 2][:, t, :, :, :], xt_low[k % 2].bitcast(F32)[:, t, :, :, :]
                ).then_inc(x_high_ready, 1)

            def split_first_high(c):
                act.wait_ge(first_xt_ready, c + 1)
                nc.scalar.copy(
                    chunk(xt_high[0], c),
                    first_banks[c][:, :].rearrange("p (b t i) -> p b t i", t=NB, i=SQ),
                ).then_inc(x_high_ready, 1)

            def load_logs():
                nc.scalar.preload_act_table_set("natural_log_exp_and_others")

            def logs(it, k, chunks=range(HC)):
                for h in chunks:
                    act.wait_ge(gate_sum_ready, quarters(it, k, h + 1))
                    nc.scalar.activation(
                        norm[:, h, :], norm[:, h, :], ACT.Ln, bias=eps[:, 0:1]
                    ).then_inc(log_sum_ready, 1)
                for h in chunks:
                    act.wait_ge(log_sum_ready, quarters(it, k, h + 1))
                    nc.scalar.activation(
                        norm[:, h, :], norm[:, h, :], ACT.Exp, scale=-1.0
                    ).then_inc(recip_ready, 1)
                for h in chunks:
                    act.wait_ge(forget_normed, quarters(it, k, h + 1))
                    nc.scalar.activation(
                        seg(log_ret, h)[:, :, 1:PAD],
                        forget[:, h, :].rearrange("p (b s) -> p b s", s=TIME),
                        ACT.Ln, bias=eps[:, 0:1],
                    ).then_inc(log_ret_ready, 1)

            def scalings(it, k, chunks=range(HC), last_group=False):
                decay = decay_of(last_group)
                if last_group:
                    act.wait_ge(hidden_ready, quarters(it, k))
                    act.wait_ge(stored[GROUPS % SLOTS], 16 * (GROUPS // SLOTS))
                else:
                    act.wait_ge(hidden_blocks_turned, quarters(it, k))
                for h in chunks:
                    act.wait_ge(cum_log_ready, quarters(it, k, h + 1))
                    cum = seg(cum_log, h)
                    nc.scalar.activation(
                        decay[:, h, :].rearrange("p (b s) -> p b s", s=TIME), cum[:, :, 1:PAD], ACT.Exp
                    )
                    for b in range(GB):
                        last = nc.scalar.activation(
                            scaled[:, h, b * TIME : (b + 1) * TIME], cum[:, b, 0:TIME],
                            ACT.Exp, bias=cum[:, b, TIME:PAD], scale=-1.0,
                        )
                    last.then_inc(scaling_ready, 1)

            def recurrence(it, k):
                load_logs()
                logs(it, k)
                scalings(it, k)

            def gates(it, k, chunks=range(HC), last_group=False):
                nc.scalar.preload_act_table_set("sigmoid_and_others")
                for h in chunks:
                    for kind, gate, ready in ((FORGET, forget, forget_ready), (INPUT, inp, input_ready)):
                        act.wait_ge(logits_ready[kind], quarters(it, k, h + 1))
                        nc.scalar.activation(
                            gate[:, h, :], bank_of(h, kind, last_group)[:, :], ACT.Sigmoid,
                            bias=bias[:, kind * HC + h : kind * HC + h + 1],
                        ).then_inc(ready, 1)
                    if not last_group and h < 3:
                        split_high(it, k + 1, h)
                    if not last_group and h == 2:
                        split_high(it, k + 1, 3)

            def weights_high(h):
                for kind in range(3):
                    n = 3 * h + kind
                    act.wait_ge(w_transposed, n + 1)
                    nc.scalar.copy(
                        wt_high[:, kind, :, h * P : (h + 1) * P],
                        w_banks[n % len(w_banks)][:, :].rearrange("p (c u) -> p c u", u=P),
                    ).then_inc(w_high_ready, 1)

            weights_high(0)
            for c in range(KC):
                split_first_high(c)
            weights_high(1)
            act.wait_ge(small_transposed, 1)
            nc.scalar.copy(bias[:, :], small_bank[:, 0 : 3 * HC]).then_inc(small_ready, 1)
            weights_high(2)
            weights_high(3)
            act.wait_ge(small_transposed, 2)
            nc.scalar.copy(cond_t[:, :, :], small_bank[:, :]).then_inc(small_ready, 1)
            act.wait_ge(small_ready, 1)
            act.wait_ge(consts_ready, 4)
            act.wait_ge(w_transposed, 3 * HC)
            gates(0, 0)
            recurrence(0, 0)
            gates(0, 1)
            with act.Fori(0, GROUPS // SLOTS - 1) as it:
                for k in range(2, SLOTS + 2):
                    recurrence(it, k - 1)
                    gates(it, k)
            last_it = GROUPS // SLOTS - 1
            recurrence(last_it, SLOTS - 3)
            gates(last_it, SLOTS - 2)
            k = SLOTS - 1
            recurrence(last_it, k - 1)
            gates(last_it, k, (0, 1), last_group=True)
            load_logs()
            logs(last_it, k, (0, 1))
            gates(last_it, k, (2, 3), last_group=True)
            load_logs()
            scalings(last_it, k, (0, 1), last_group=True)
            logs(last_it, k, (2, 3))
            scalings(last_it, k, (2, 3), last_group=True)

        @block.vector
        def _(dve):
            def turn_blocks(it, k, b):
                if b == 0:
                    s = k % SLOTS
                    dve.wait_ge(x_loaded[s], it * 16 + 16 * (k // SLOTS + 1))
                    dve.wait_ge(x_high_ready, quarters(it, k))
                nc.vector.transpose(
                    x_turned[:, :, b, :, :].rearrange("p a c i -> p c a i"),
                    x_tile[k % SLOTS][:, b, :].rearrange("p (c a d) -> p c a d", c=KC, d=SQ),
                ).then_inc(blocks_turned, 1)

            def split_first_low(c):
                dve.wait_ge(x_high_ready, c + 1)
                nc.vector.tensor_tensor(
                    chunk(xt_low[0], c),
                    first_banks[c][:, :].rearrange("p (b t i) -> p b t i", t=NB, i=SQ),
                    chunk(xt_high[0].bitcast(F32), c), ALU.subtract,
                ).then_inc(x_low_ready, 1)

            def gate_candidate(it, k, h):
                dve.wait_ge(input_ready, quarters(it, k, h + 1))
                dve.wait_ge(logits_ready[CAND], quarters(it, k, h + 1))
                nc.vector.scalar_tensor_tensor(
                    info[:, h, :], logit_bank[h % 2][CAND][:, :],
                    bias[:, CAND * HC + h : CAND * HC + h + 1], inp[:, h, :], ALU.add, ALU.mult,
                ).then_inc(cand_gated, 1)

            def norm_forget(it, k, h):
                dve.wait_ge(recip_ready, quarters(it, k, h + 1))
                nc.vector.tensor_tensor(
                    forget[:, h, :], forget[:, h, :], norm[:, h, :], ALU.mult
                ).then_inc(forget_normed, 1)

            def sum_logs(it, k, h):
                dve.wait_ge(log_ret_ready, quarters(it, k, h + 1))
                nc.vector.tensor_tensor_scan(
                    cum_log[:, h, :], keep_pad[:, :], log_ret[:, h, :], 0.0, ALU.mult, ALU.add
                ).then_inc(cum_log_ready, 1)

            def scale_info(it, k, h):
                dve.wait_ge(scaling_ready, quarters(it, k, h + 1))
                dve.wait_ge(info_ready, quarters(it, k, h + 1))
                nc.vector.tensor_tensor(
                    info[:, h, :], info[:, h, :], scaled[:, h, :], ALU.mult
                ).then_inc(info_scaled, 1)

            def sum_info(it, k, h):
                dve.wait_ge(info_scaled, quarters(it, k, h + 1))
                nc.vector.tensor_tensor_scan(
                    scaled[:, h, :], keep[:, :], info[:, h, :], 0.0, ALU.mult, ALU.add
                ).then_inc(info_summed, 1)

            def add_initial(it, k, h, last_group=False):
                decay = decay_of(last_group)
                dve.wait_ge(info_summed, quarters(it, k, h + 1))
                for b in range(GB):
                    t = slice(b * TIME, (b + 1) * TIME)
                    last = nc.vector.scalar_tensor_tensor(
                        decay[:, h, t], decay[:, h, t], cond_group[:, h, b : b + 1],
                        scaled[:, h, t], ALU.mult, ALU.add,
                    )
                last.then_inc(hidden_ready, 1)

            def add_x(k, b, source):
                dve.wait_ge(ht_ready, quarters(0, k - (SLOTS - 2), b + 1))
                nc.vector.tensor_tensor(
                    x_tile[k % SLOTS][:, b, :], source[:, :], x_tile[k % SLOTS][:, b, :], ALU.add
                ).then_inc(out_ready, 1)

            def turn_hidden(it, k, h):
                dve.wait_ge(hidden_ready, quarters(it, k, h + 1))
                nc.vector.transpose(
                    hidden_turned[:, :, :, h, :].rearrange("p t b j -> p b t j"),
                    decay[:, h, :].rearrange("p (b t i) -> p b t i", t=NB, i=SQ),
                ).then_inc(hidden_blocks_turned, 1)

            def add_moved(it, k, b):
                if b == 0:
                    n = 16 * NB * NB
                    dve.wait_ge(hidden_blocks_moved[k % 2], it * (2 * n) + n * (k // 2 + 1))
                rows = x_tile[k % SLOTS][:, b, :].rearrange("p (h u j) -> p h u j", h=HC, j=SQ)
                nc.vector.tensor_tensor(
                    rows, hidden_moved[:, :, b, :, :].rearrange("p u h j -> p h u j"), rows, ALU.add
                ).then_inc(out_ready, 1)

            def period(it, k, first=False, last=False, more=True):
                for h in range(HC):
                    norm_forget(it, k - 1, h)
                for h in range(HC):
                    sum_logs(it, k - 1, h)
                if not first:
                    for b in range(GB):
                        add_moved(it, k - 2, b)
                dve.wait_ge(cond_group_ready, it * SLOTS + k)
                scale_info(it, k - 1, 0)
                scale_info(it, k - 1, 1)
                sum_info(it, k - 1, 0)
                sum_info(it, k - 1, 1)
                add_initial(it, k - 1, 0)
                scale_info(it, k - 1, 2)
                gate_candidate(it, k, 0)
                add_initial(it, k - 1, 1)
                sum_info(it, k - 1, 2)
                if last:
                    norm_forget(it, k, 0)
                    norm_forget(it, k, 1)
                scale_info(it, k - 1, 3)
                sum_info(it, k - 1, 3)
                gate_candidate(it, k, 1)
                add_initial(it, k - 1, 2)
                add_initial(it, k - 1, 3)
                if last:
                    last_recurrence(it, k)
                    return
                for h in range(HC):
                    turn_hidden(it, k - 1, h)
                gate_candidate(it, k, 2)
                if more:
                    for b in range(GB):
                        turn_blocks(it, k + 2, b)
                gate_candidate(it, k, 3)

            def last_recurrence(it, k):

                def add_before(b):
                    add_x(k - 1, b, spare_bank[b % 2])

                def finish(h):
                    scale_info(it, k, h)
                    sum_info(it, k, h)
                    add_initial(it, k, h, last_group=True)

                sum_logs(it, k, 0)
                sum_logs(it, k, 1)
                add_before(0)
                dve.wait_ge(cond_group_ready, it * SLOTS + (k + 1))
                finish(0)
                gate_candidate(it, k, 2)
                finish(1)
                norm_forget(it, k, 2)
                norm_forget(it, k, 3)
                add_before(1)
                gate_candidate(it, k, 3)
                sum_logs(it, k, 2)
                sum_logs(it, k, 3)
                add_before(2)
                add_before(3)
                finish(2)
                finish(3)

            nc.vector.memset(keep_pad[:, :], 1.0).then_inc(consts_ready, 1)
            nc.vector.memset(keep[:, :], 1.0).then_inc(consts_ready, 1)
            nc.vector.memset(eps[:, :], EPS).then_inc(consts_ready, 1)
            nc.vector.memset(
                log_ret[:, :, :].rearrange("p h (b s) -> p (h b) s", s=PAD)[:, :, 0:1], 0.0
            ).then_inc(consts_ready, 1)
            dve.wait_ge(consts_ready, 2)
            nc.vector.memset(
                keep_pad[:, :].rearrange("p (b s) -> p b s", s=PAD)[:, :, 0:1], 0.0
            ).then_inc(consts_ready, 1)
            nc.vector.memset(
                keep[:, :].rearrange("p (b s) -> p b s", s=TIME)[:, :, 0:1], 0.0
            ).then_inc(consts_ready, 1)

            def weights_low(h):
                for kind in range(3):
                    n = 3 * h + kind
                    dve.wait_ge(w_high_ready, n + 1)
                    w = (slice(None), kind, slice(None), slice(h * P, (h + 1) * P))
                    nc.vector.tensor_tensor(
                        wt_low[w], w_banks[n % len(w_banks)][:, :].rearrange("p (c u) -> p c u", u=P),
                        wt_high[w].bitcast(F32), ALU.subtract,
                    ).then_inc(w_low_ready, 1)

            weights_low(0)
            for c in range(KC):
                split_first_low(c)
            for h in range(1, HC):
                weights_low(h)
            for b in range(GB):
                turn_blocks(0, 1, b)
            dve.wait_ge(consts_ready, 6)
            dve.wait_ge(small_ready, 1)
            for h in range(HC):
                gate_candidate(0, 0, h)
                if h == HC - 2:
                    for b in range(GB):
                        turn_blocks(0, 2, b)
            period(0, 1, first=True)
            with dve.Fori(0, GROUPS // SLOTS - 1) as it:
                for k in range(2, SLOTS + 2):
                    period(it, k)
            last_it = GROUPS // SLOTS - 1
            period(last_it, 2, more=False)
            period(last_it, 3, last=True)
            for b in range(GB):
                add_x(SLOTS - 1, b, last_banks[b])

        @block.tensor
        def _(pe):
            def transpose_first_x(c):
                for b in range(GB):
                    last = nc.tensor.transpose(
                        first_banks[c][:, b * TIME : (b + 1) * TIME],
                        x_tile[0][:, b, c * P : (c + 1) * P], ident[:, :],
                    )
                last.then_inc(first_xt_ready, 1)

            def transpose_hidden(it, k, b):
                if b == 0:
                    pe.wait_ge(hidden_ready, quarters(it, k, HC))
                if b >= 2:
                    pe.wait_ge(out_ready, quarters(it, k, b - 1))
                for h in range(HC):
                    last = nc.tensor.transpose(
                        spare_bank[b % 2][:, h * P : (h + 1) * P],
                        decay[:, h, b * TIME : (b + 1) * TIME], ident[:, :],
                    )
                last.then_inc(ht_ready, 1)

            def project(it, k, h, kind, first=False, last_group=False):
                if h == 0 and kind == FORGET:
                    pe.wait_ge(x_low_ready, quarters(it, k, KC))
                if first and h == 0:
                    pe.wait_ge(w_low_ready, kind + 1)
                if first and h == 1:
                    pe.wait_ge(w_low_ready, 3 * HC)
                if first and h == 2 and kind == FORGET:
                    pe.wait_ge(small_ready, 2)
                back = 2 if kind == CAND or last_group else (4, 2, 4, 2)[h]
                if not first or h >= back:
                    freed = (forget_ready, input_ready, cand_gated)[kind]
                    pe.wait_ge(freed, quarters(it, k, h - back + 1))
                high, low = xt_high[k % 2], xt_low[k % 2]
                units = slice(h * P, (h + 1) * P)
                for c in range(KC):
                    for n, (w, xt) in enumerate(((wt_high, high), (wt_high, low), (wt_low, high))):
                        last = nc.tensor.matmul(
                            bank_of(h, kind, last_group)[:, :], w[:, kind, c, units], chunk(xt, c),
                            start=c == 0 and n == 0, stop=c == KC - 1 and n == 2,
                        )
                last.then_inc(logits_ready[kind], 1)

            def period(it, k):
                for h in range(HC):
                    for kind in (FORGET, INPUT, CAND):
                        project(it, k, h, kind)

            def transpose_weights(h):
                pe.wait_ge(w_loaded[h], 48)
                for kind in range(3):
                    n = 3 * h + kind
                    if n >= len(w_banks):
                        pe.wait_ge(w_low_ready, n - len(w_banks) + 1)
                    for c in range(KC):
                        last = nc.tensor.transpose(
                            w_banks[n % len(w_banks)][:, c * P : (c + 1) * P],
                            w_rows[kind][:, h, c * P : (c + 1) * P], ident[:, :],
                        )
                    last.then_inc(w_transposed, 1)

            pe.wait_ge(ident_ready, 1)
            transpose_weights(0)
            pe.wait_ge(x_loaded[0], 16)
            for c in range(KC):
                transpose_first_x(c)
            transpose_weights(1)
            pe.wait_ge(x_low_ready, KC)
            pe.wait_ge(small_loaded[0], 48)
            nc.tensor.transpose(
                small_bank[:, 0 : 3 * HC], bias_rows[:, :], ident[0 : 3 * HC, 0 : 3 * HC]
            ).then_inc(small_transposed, 1)
            project(0, 0, 0, FORGET, first=True)
            transpose_weights(2)
            project(0, 0, 0, INPUT, first=True)
            transpose_weights(3)
            pe.wait_ge(small_loaded[1], 16)
            pe.wait_ge(small_ready, 1)
            for h in range(HC):
                last = nc.tensor.transpose(
                    small_bank[:, h * BATCH : (h + 1) * BATCH],
                    cond_rows[:, h * P : (h + 1) * P], ident[:, :],
                )
            last.then_inc(small_transposed, 1)
            project(0, 0, 0, CAND, first=True)
            for h in range(1, HC):
                project(0, 0, h, FORGET, first=True)
                project(0, 0, h, INPUT, first=True)
                project(0, 0, h, CAND, first=True)
            period(0, 1)
            with pe.Fori(0, GROUPS // SLOTS - 1) as it:
                for k in range(2, SLOTS + 2):
                    period(it, k)
            last_it = GROUPS // SLOTS - 1
            period(last_it, 2)
            k = SLOTS - 1
            for h in range(2):
                for kind in (FORGET, INPUT, CAND):
                    project(last_it, k, h, kind, last_group=True)
            project(last_it, k, 2, FORGET, last_group=True)
            project(last_it, k, 2, INPUT, last_group=True)
            project(last_it, k, 3, FORGET, last_group=True)
            project(last_it, k, 3, INPUT, last_group=True)
            transpose_hidden(last_it, k - 1, 0)
            transpose_hidden(last_it, k - 1, 1)
            project(last_it, k, 2, CAND, last_group=True)
            project(last_it, k, 3, CAND, last_group=True)
            transpose_hidden(last_it, k - 1, 2)
            transpose_hidden(last_it, k - 1, 3)
            pe.wait_ge(cand_gated, quarters(last_it, k, HC))
            pe.wait_ge(out_ready, quarters(last_it, k))
            for h in range(HC):
                if h >= HC - 2:
                    pe.wait_ge(hidden_ready, quarters(last_it, k, h + 1))
                elif h == 0:
                    pe.wait_ge(hidden_ready, quarters(last_it, k, HC - 2))
                for b in range(GB):
                    last = nc.tensor.transpose(
                        last_banks[b][:, h * P : (h + 1) * P],
                        last_decay[:, h, b * TIME : (b + 1) * TIME], ident[:, :],
                    )
                    if h == HC - 1:
                        last.then_inc(ht_ready, 1)


_INS = ["x", "cond_1024", "L0_cond_W_f", "L0_cond_b_f", "L0_cond_W_i", "L0_cond_b_i", "L0_cond_W_h", "L0_cond_b_h"]


def kernel(**inputs):
    import numpy as _np
    import concourse.bacc as _bacc
    from concourse import mybir as _mybir
    from concourse.bass_utils import run_bass_kernel_spmd as _run

    nc = _bacc.Bacc("TRN2", target_bir_lowering=False, num_devices=1)
    arrays, args = {}, []
    for name in _INS:
        a = _np.ascontiguousarray(inputs[name])
        arrays[f"in_{name}_dram"] = a
        args.append(nc.dram_tensor(f"in_{name}_dram", a.shape, _mybir.dt.from_np(a.dtype), kind="ExternalInput").ap())
    args.append(nc.dram_tensor("out_0_dram", (BATCH, TIME, DIM), F32, kind="ExternalOutput").ap())
    build(nc, *args)
    r = _run(nc, [arrays], core_ids=[0])
    return r.results[0]["out_0_dram"]
```
